# Optimizing a Trainium2 kernel written in Bass

```python
import numpy as np
import jax
import jax.numpy as jnp

def _softmax(x, axis=-1):
    return jax.nn.softmax(x, axis=axis)

def _gelu(x):
    return jax.nn.gelu(x, approximate=True)

def _silu(x):
    return jax.nn.silu(x)

def _sigmoid(x):
    return jax.nn.sigmoid(x)

def _layernorm(x, axis=-1, eps=1e-05):
    m = jnp.mean(x, axis=axis, keepdims=True)
    v = jnp.var(x, axis=axis, keepdims=True)
    return (x - m) / jnp.sqrt(v + eps)

def _scatter_add(tgt, idx, src, axis=0):
    return tgt.at[idx].add(src)

def _segment_sum(src, seg, n):
    return jax.ops.segment_sum(src, seg, n)
kernel_name = 'mk_prb_d1_jaxref_r8_554655'

def setup_inputs(seed: int=0):
    np.random.seed(seed)
    _w = jnp.asarray

    def _L0_attn_setup():
        import jax, jax.numpy as jnp
        import numpy as np
        EPS = 1e-05
        key = jax.random.key(seed)
        ks = jax.random.split(key, 6)
        B, T, H = (4, 256, 256)
        scale = 2 ** (-2.5) * (6.0 / (H + H)) ** 0.5
        return {'hidden_states': jax.random.normal(ks[0], (B, T, H), dtype=jnp.float32), 'Wi': jax.random.normal(ks[1], (H, H), dtype=jnp.float32) * scale, 'Wf': jax.random.normal(ks[2], (H, H), dtype=jnp.float32) * scale, 'Wg': jax.random.normal(ks[3], (H, H), dtype=jnp.float32) * scale, 'Wo': jax.random.normal(ks[4], (H, H), dtype=jnp.float32) * scale, 'gnorm_w': jnp.ones((H,), dtype=jnp.float32)}
    _L0_attn_in = _L0_attn_setup()

    def _L0_ffn_setup():
        import jax, jax.numpy as jnp
        import numpy as np
        H = 256
        I = 128
        K = 8
        E = 128
        TOPK = 4
        EPS = 1e-08
        key = jax.random.key(seed)
        ks = jax.random.split(key, 10)
        s = 0.02
        return {'x': jax.random.normal(ks[0], (4, 256, H), jnp.float32), 'w_router': jax.random.normal(ks[1], (H, E), jnp.float32) * s, 'w_gate': jax.random.normal(ks[2], (H, K * I), jnp.float32) * s, 'w_up': jax.random.normal(ks[3], (H, K * I), jnp.float32) * s, 'w_down': jax.random.normal(ks[4], (I, H), jnp.float32) * s, 'amplitudes': jax.random.normal(ks[5], (E, K, 2), jnp.float32) * 0.1, 'expert_scale': jnp.ones((E,), jnp.float32), 'shared_w_gate': jax.random.normal(ks[6], (H, 2 * I), jnp.float32) * s, 'shared_w_up': jax.random.normal(ks[7], (H, 2 * I), jnp.float32) * s, 'shared_w_down': jax.random.normal(ks[8], (2 * I, H), jnp.float32) * s}
    _L0_ffn_in = _L0_ffn_setup()
    _d = {'L0_attn_hidden_states': _L0_attn_in['hidden_states'], 'L0_attn_Wi': _L0_attn_in['Wi'], 'L0_attn_Wf': _L0_attn_in['Wf'], 'L0_attn_Wg': _L0_attn_in['Wg'], 'L0_attn_Wo': _L0_attn_in['Wo'], 'L0_attn_gnorm_w': _L0_attn_in['gnorm_w'], 'L0_ffn_w_router': _L0_ffn_in['w_router'], 'L0_ffn_w_gate': _L0_ffn_in['w_gate'], 'L0_ffn_w_up': _L0_ffn_in['w_up'], 'L0_ffn_w_down': _L0_ffn_in['w_down'], 'L0_ffn_amplitudes': _L0_ffn_in['amplitudes'], 'L0_ffn_expert_scale': _L0_ffn_in['expert_scale'], 'L0_ffn_shared_w_gate': _L0_ffn_in['shared_w_gate'], 'L0_ffn_shared_w_up': _L0_ffn_in['shared_w_up'], 'L0_ffn_shared_w_down': _L0_ffn_in['shared_w_down']}
    _x0 = _d['L0_attn_hidden_states']
    _d['L0_attn_hidden_states'] = jax.random.normal(jax.random.fold_in(jax.random.key(seed), 1), (4, 512, 256), dtype=_x0.dtype)
    del _x0
    return _d

def reference(L0_attn_hidden_states, L0_attn_Wi, L0_attn_Wf, L0_attn_Wg, L0_attn_Wo, L0_attn_gnorm_w, L0_ffn_w_router, L0_ffn_w_gate, L0_ffn_w_up, L0_ffn_w_down, L0_ffn_amplitudes, L0_ffn_expert_scale, L0_ffn_shared_w_gate, L0_ffn_shared_w_up, L0_ffn_shared_w_down):

    def _L0_attn_ref(hidden_states, Wi, Wf, Wg, Wo, gnorm_w):
        import jax, jax.numpy as jnp
        import numpy as np
        EPS = 1e-05
        i = jnp.einsum('bth,dh->btd', hidden_states, Wi)
        f = jnp.einsum('bth,dh->btd', hidden_states, Wf)
        g = jnp.einsum('bth,dh->btd', hidden_states, Wg)
        gate = jax.nn.sigmoid(f)
        v = jax.nn.silu(i) * (1.0 - gate)

        def combine(c1, c2):
            a1, b1 = c1
            a2, b2 = c2
            return (a1 * a2, a2 * b1 + b2)
        _, o = jax.lax.associative_scan(combine, (gate, v), axis=1)
        rms = o * jax.lax.rsqrt(jnp.mean(o * o, axis=-1, keepdims=True) + EPS)
        o = rms * gnorm_w * g * jax.nn.sigmoid(g)
        return jnp.einsum('btd,hd->bth', o, Wo)

    def _L0_ffn_ref(x, w_router, w_gate, w_up, w_down, amplitudes, expert_scale, shared_w_gate, shared_w_up, shared_w_down):
        import jax, jax.numpy as jnp
        import numpy as np
        H = 256
        I = 128
        K = 8
        E = 128
        TOPK = 4
        EPS = 1e-08
        B, S, _ = x.shape
        T = B * S
        xt = x.reshape(T, H)
        probs = jax.nn.softmax(xt @ w_router, axis=-1)
        topk_p, topk_idx = jax.lax.top_k(probs, TOPK)
        topk_w = topk_p / (jnp.sum(topk_p, axis=-1, keepdims=True) + EPS)
        gate = (xt @ w_gate).reshape(T, K, I)
        up = (xt @ w_up).reshape(T, K, I)
        basis = jax.nn.silu(gate) * up
        p = amplitudes[..., 0] ** 2 + amplitudes[..., 1] ** 2
        mix = p / (jnp.sum(p, axis=-1, keepdims=True) + EPS)
        mix_sel = mix[topk_idx]
        mixed = jnp.einsum('tek,tki->tei', mix_sel, basis)
        down = jnp.einsum('tei,ih->teh', mixed, w_down)
        coeff = topk_w * expert_scale[topk_idx]
        out = jnp.einsum('teh,te->th', down, coeff)
        shared = jax.nn.silu(xt @ shared_w_gate) * (xt @ shared_w_up) @ shared_w_down
        out = out + shared
        return out.reshape(B, S, H)
    x = L0_attn_hidden_states
    xn = _layernorm(x, axis=-1)
    x = x + _L0_attn_ref(xn, L0_attn_Wi, L0_attn_Wf, L0_attn_Wg, L0_attn_Wo, L0_attn_gnorm_w) + _L0_ffn_ref(xn, L0_ffn_w_router, L0_ffn_w_gate, L0_ffn_w_up, L0_ffn_w_down, L0_ffn_amplitudes, L0_ffn_expert_scale, L0_ffn_shared_w_gate, L0_ffn_shared_w_up, L0_ffn_shared_w_down)
    return x

_drawn_inputs = setup_inputs


def setup_inputs(seed=0):
    import zlib

    import numpy as np

    out = dict(_drawn_inputs(seed))
    spreads = {'L0_attn_gnorm_w': (1.0, 0.6), 'L0_ffn_expert_scale': (1.0, 0.6)}
    factors = {'L0_attn_Wf': 37.966,
     'L0_ffn_w_router': 8.0,
     'L0_ffn_w_gate': 8.0,
     'L0_ffn_w_up': 8.0,
     'L0_ffn_w_down': 8.0,
     'L0_ffn_amplitudes': 8.0,
     'L0_ffn_shared_w_gate': 3.417,
     'L0_ffn_shared_w_up': 3.384,
     'L0_ffn_shared_w_down': 3.37,
     'L0_attn_Wi': 3.455,
     'L0_attn_Wg': 3.437,
     'L0_attn_Wo': 3.354}
    for name, (base, spread) in spreads.items():
        noise = np.random.default_rng([zlib.crc32(name.encode()), seed]).standard_normal(out[name].shape)
        drawn = base * np.exp(spread * noise) if base else spread * noise
        out[name] = jnp.asarray(drawn.astype(out[name].dtype))
    for name, factor in factors.items():
        out[name] = (out[name] * factor).astype(out[name].dtype)
    return out
```

```python
from contextlib import ExitStack

import concourse.bass as bass
from concourse import mybir

P = 128


def layer_kernel(nc, x, router_w, rec_w, shared_w, routed_w, down_w, gnorm, amps, escale, out):
    fp32 = mybir.dt.float32
    fp32r = mybir.dt.float32r
    ALU = mybir.AluOpType
    ACT = mybir.ActivationFunctionType
    AX = mybir.AxisListType

    NB, T, H = x.shape
    NT = T // P
    KC = H // P
    DC = H // P
    NE = amps.shape[0]
    NK = amps.shape[1] // 2
    TOPK = 4
    UK = NK // 2
    FW = UK * P
    NU = 2
    NQ = TOPK * 2
    LW = NE + NQ - TOPK
    PAD = -3.0e38
    MARK = 3.0e38
    LN_EPS, RMS_EPS, FFN_EPS = 1e-5, 1e-5, 1e-8
    PAIRS = NB // 2
    assert PAIRS == 2 and NT == 4 and KC == 2 and DC == 2 and NE == P and T == 512

    ctx = ExitStack()
    with ctx:
        def sb(name, shape, dt=fp32):
            return ctx.enter_context(nc.sbuf_tensor(name, shape, dt))

        def pb(name):
            return ctx.enter_context(nc.psum_tensor(name, [P, 512], fp32))

        def sem(name):
            return ctx.enter_context(nc.semaphore(name))

        ident = sb("ident", [P, P])
        router_sb = sb("router_sb", [P, KC, NE])
        rec_st = sb("rec_st", [P, 3, KC, H])
        rec_hi = sb("rec_hi", [P, 3, KC, H], fp32r)
        rec_lo = sb("rec_lo", [P, 3, KC, H], fp32r)
        sha_st = sb("sha_st", [P, KC, 2 * H])
        sha_hi = sb("sha_hi", [P, KC, 2 * H], fp32r)
        sha_lo = sb("sha_lo", [P, KC, 2 * H], fp32r)
        rou_st = sb("rou_st", [P, 2 * NU, KC, FW])
        rou_hi = sb("rou_hi", [P, 2 * NU, KC, FW], fp32r)
        rou_lo = sb("rou_lo", [P, 2 * NU, KC, FW], fp32r)
        down_sb = sb("down_sb", [P, 2 * DC + 1, H])
        gnorm_sb = sb("gnorm_sb", [P, DC])
        amps_sb = sb("amps_sb", [P, NK, 2])
        escale_sb = sb("escale_sb", [P, 1])
        amp2 = sb("amp2", [P, NK, 2])
        power = sb("power", [P, NK])
        psum_all = sb("psum_all", [P, 1])
        pinv = sb("pinv", [P, 1])
        escaled = sb("escaled", [P, 1])
        mixw = sb("mixw", [P, NK + 1])
        ones = sb("ones", [P, 1])
        neghalf = sb("neghalf", [P, NT])

        x_sb = [sb(f"x_sb{p}", [P, NT, H]) for p in range(2)]
        bn = sb("bn", [P, NT, 6])
        mv = sb("mv", [P, NT, 2])
        negmean = sb("negmean", [P, NT])
        vareps = sb("vareps", [P, NT])
        rstd = sb("rstd", [P, NT])
        xn = sb("xn", [P, NT, H])
        xT_hi = [sb(f"xT_hi{p}", [P, KC, T], fp32r) for p in range(2)]
        xT_lo = [sb(f"xT_lo{p}", [P, KC, T], fp32r) for p in range(2)]
        xT = sb("xT", [P, KC, T])
        logits = sb("logits", [P, NT, LW])
        marked = sb("marked", [P, NT, LW])
        top8 = sb("top8", [P, NT, NQ])
        keys = sb("keys", [P, NT, NQ])
        negmax = sb("negmax", [P, NT])
        expd = sb("expd", [P, NT, NE])
        expsum = sb("expsum", [P, NT])
        chosen = sb("chosen", [P, NT, NE])
        chosenT = sb("chosenT", [P, T])
        den = sb("den", [P, NT])
        deninv = sb("deninv", [P, NT])
        coef = sb("coef", [P, NT, NK])
        th = sb("th", [P, DC, T])
        decay = sb("decay", [P, DC, T])
        si = sb("si", [P, DC, T])
        inflow = sb("inflow", [P, DC, T])
        state = sb("state", [P, DC, T])
        state2 = sb("state2", [P, DC, T])
        gs = sb("gs", [P, DC, T])
        gated = sb("gated", [P, DC, T])
        meansq = sb("meansq", [P, NT])
        rpow = sb("rpow", [P, NT])
        rscale = sb("rscale", [P, NT])
        sha_act = sb("sha_act", [P, DC, T])
        sha = sb("sha", [P, DC, T])
        act = [sb(f"act{u}", [P, FW]) for u in range(NU)]
        basis = [sb(f"basis{u}", [P, FW]) for u in range(NU)]
        mixed = [sb(f"mixed{j}", [P, P]) for j in range(2)]
        mixedT = sb("mixedT", [P, P])
        out_sb = [sb(f"out_sb{j}", [P, H]) for j in range(NT)]

        wide = [pb("wide0"), pb("wide1")]
        gate_ps = [pb(f"gate_ps{u}") for u in range(NU)]
        up_ps = [pb(f"up_ps{u}") for u in range(NU)]
        aux = pb("aux")
        proj = pb("proj")

        x_loaded = [sem(f"x_loaded{p}") for p in range(2)]
        router_loaded = sem("router_loaded")
        rec_loaded = [sem(f"rec_loaded{w}") for w in range(3)]
        sha_loaded = sem("sha_loaded")
        rou_loaded = [sem(f"rou_loaded{w}") for w in range(2 * NU)]
        down_loaded = sem("down_loaded")
        small_loaded = [sem(f"small_loaded{w}") for w in range(3)]
        consts_ready = sem("consts_ready")
        ident_ready = sem("ident_ready")
        neghalf_ready = sem("neghalf_ready")
        waited_apart = sem("waited_apart")
        rechi_ready = sem("rechi_ready")
        reclo_ready = sem("reclo_ready")
        rouhi_ready = sem("rouhi_ready")
        roulo_ready = sem("roulo_ready")
        mixw_steps = sem("mixw_steps")
        bn_ready = sem("bn_ready")
        mv_ready = sem("mv_ready")
        ln_steps = sem("ln_steps")
        xn_ready = sem("xn_ready")
        xhi_ready = sem("xhi_ready")
        xlo_ready = sem("xlo_ready")
        xT_ready = sem("xT_ready")
        wide_ready = [sem("wide0_ready"), sem("wide1_ready")]
        aux_ready = sem("aux_ready")
        logits_ready = sem("logits_ready")
        top8_ready = sem("top8_ready")
        keys_ready = sem("keys_ready")
        negmax_ready = sem("negmax_ready")
        marked_ready = sem("marked_ready")
        exp_ready = sem("exp_ready")
        chosen_ready = sem("chosen_ready")
        chosenT_ready = sem("chosenT_ready")
        den_ready = sem("den_ready")
        deninv_ready = sem("deninv_ready")
        coef_ready = sem("coef_ready")
        th_ready = sem("th_ready")
        decay_ready = sem("decay_ready")
        si_ready = sem("si_ready")
        inflow_ready = sem("inflow_ready")
        state_ready = sem("state_ready")
        state2_ready = sem("state2_ready")
        gs_ready = sem("gs_ready")
        gated_ready = sem("gated_ready")
        meansq_ready = sem("meansq_ready")
        rpow_ready = sem("rpow_ready")
        rscale_ready = sem("rscale_ready")
        shaact_ready = sem("shaact_ready")
        sha_ready = sem("sha_ready")
        gate_ready = [sem(f"gate_ready{u}") for u in range(NU)]
        up_ready = [sem(f"up_ready{u}") for u in range(NU)]
        act_ready = [sem(f"act_ready{u}") for u in range(NU)]
        basis_ready = [sem(f"basis_ready{u}") for u in range(NU)]
        mix_steps = sem("mix_steps")
        mixedT_ready = sem("mixedT_ready")
        proj_ready = sem("proj_ready")
        resid_ready = sem("resid_ready")
        out_ready = sem("out_ready")
        out_stored = [sem(f"out_stored{j}") for j in range(NT)]

        def count(i, p, n, k):
            return i * (2 * n) + (p * n + k)

        MIX = NK * NT
        WIDE = 6
        AUX = 8
        X_USE = 0
        CHOSEN_USE, COEF_USE, SUMSQ_USE, MIX0_USE, ROUTER_USE, MIX3_USE = 1, 2, 3, 4, 7, 8

        def aux_at(i, p, use):
            return count(i, p, AUX, 1 + use)

        def mix_use(j):
            return MIX3_USE if j == NT - 1 else MIX0_USE + j

        x_v = x.rearrange("b (j p) h -> b p j h", p=P)
        out_v = out.rearrange("b (j p) h -> b j p h", p=P)

        def wait_apart(eng, semaphore, value):
            eng.wait_ge(semaphore, value)
            eng.sem_inc(waited_apart, 1)

        block = ctx.enter_context(nc.Block())

        @block.sync
        def _(sp):
            for j in range(NT):
                sp.sem_inc(out_stored[j], 16)
            sp.dma_start(x_sb[0][:], x_v[0]).then_inc(x_loaded[0], 16)
            for w in range(3):
                sp.dma_start(rec_st[:, w], rec_w[w]).then_inc(rec_loaded[w], 16)
            sp.dma_start(sha_st[:], shared_w).then_inc(sha_loaded, 16)
            for w in range(2 * NU):
                sp.dma_start(rou_st[:, w], routed_w[w]).then_inc(rou_loaded[w], 16)
            sp.dma_start(down_sb[:], down_w).then_inc(down_loaded, 16)
            with sp.Fori(0, PAIRS) as i:
                for p in range(2):
                    sp.wait_ge(gated_ready, count(i, p, DC, 1))
                    nxt = i * 2 + 1 if p == 0 else (i * -2) + (NB - 2)
                    sp.dma_start(x_sb[1 - p][:], x_v[nxt]).then_inc(x_loaded[1 - p], 16)
                    for j in range(NT):
                        sp.wait_ge(out_ready, count(i, p, NT, j + 1))
                        sp.dma_start(out_v[i * 2 + p, j], out_sb[j][:]).then_inc(out_stored[j], 16)
            for j in range(NT):
                sp.wait_ge(out_stored[j], 16 * (NB + 1))
            sp.wait_ge(x_loaded[0], 16 * (PAIRS + 1))

        @block.gpsimd
        def _(pool):
            nc.gpsimd.dma_start(amps_sb[:], amps.rearrange("e (k c) -> e k c", c=2)).then_inc(small_loaded[0], 16)
            nc.gpsimd.dma_start(escale_sb[:], escale).then_inc(small_loaded[1], 16)
            nc.gpsimd.dma_start(gnorm_sb[:], gnorm).then_inc(small_loaded[2], 16)
            nc.gpsimd.memset(ident[:], 0.0).then_inc(ident_ready, 1)
            nc.gpsimd.memset(neghalf[:], -0.5).then_inc(neghalf_ready, 1)
            pool.wait_ge(ident_ready, 1)
            nc.gpsimd.affine_select(out=ident[:], in_=ident[:], compare_op=ALU.not_equal, fill=1.0, base=0,
                                    pattern=[[-1, P]], channel_multiplier=1).then_inc(ident_ready, 1)
            pool.wait_ge(neghalf_ready, 1)

            def normalise(i, q):
                wait_apart(pool, mv_ready, count(i, q, NT, NT))
                nc.gpsimd.tensor_scalar(negmean[:], mv[:, :, 0], -1.0, 0.0, ALU.mult, ALU.add).then_inc(ln_steps, 1)
                nc.gpsimd.tensor_scalar(vareps[:], mv[:, :, 1], 1.0, LN_EPS, ALU.mult, ALU.add).then_inc(ln_steps, 1)
                pool.wait_ge(ln_steps, count(i, q, 3, 2))
                nc.gpsimd.tensor_tensor(rstd[:], vareps[:], neghalf[:], ALU.pow).then_inc(ln_steps, 1)
                wait_apart(pool, ln_steps, count(i, q, 3, 3))
                for j in range(NT):
                    nc.gpsimd.tensor_scalar(xn[:, j], x_sb[q % 2][:, j], negmean[:, j:j + 1], rstd[:, j:j + 1],
                                            ALU.add, ALU.mult).then_inc(xn_ready, 1)

            def join(i, q):
                for h in range(2):
                    pool.wait_ge(xlo_ready, count(i, q, 2, h + 1))
                    s = slice(h * T // 2, (h + 1) * T // 2)
                    nc.gpsimd.tensor_tensor(xT[:, :, s], xT_hi[q % 2][:, :, s].bitcast(fp32),
                                            xT_lo[q % 2][:, :, s].bitcast(fp32), ALU.add).then_inc(xT_ready, 1)

            normalise(0, 0)
            join(0, 0)
            for w in range(2 * NU):
                pool.wait_ge(rou_loaded[w], 16)
                nc.gpsimd.tensor_scalar(rou_hi[:, w], rou_st[:, w], 1.0, 0.0, ALU.mult, ALU.add).then_inc(rouhi_ready, 1)
                pool.wait_ge(rouhi_ready, w + 1)
                nc.gpsimd.tensor_tensor(rou_lo[:, w], rou_st[:, w], rou_hi[:, w].bitcast(fp32),
                                        ALU.subtract).then_inc(roulo_ready, 1)
            with pool.Fori(0, PAIRS) as i:
                for p in range(2):
                    pool.wait_ge(meansq_ready, count(i, p, 1, 1))
                    nc.gpsimd.tensor_tensor(rpow[:], meansq[:], neghalf[:], ALU.pow).then_inc(rpow_ready, 1)
                    wait_apart(pool, rpow_ready, count(i, p, 1, 1))
                    nc.gpsimd.tensor_scalar(rscale[:], rpow[:], -0.5, 0.0, ALU.mult, ALU.add).then_inc(rscale_ready, 1)
                    normalise(i, p + 1)
                    join(i, p + 1)

        @block.scalar
        def _(sc):
            sc.dma_start(router_sb[:], router_w).then_inc(router_loaded, 16)

            def high(i, q):
                for h in range(2):
                    sc.wait_ge(wide_ready[h], count(i, q, WIDE, X_USE + 1))
                    nc.scalar.activation(xT_hi[q % 2][:, :, h * T // 2:(h + 1) * T // 2],
                                         wide[h][:].rearrange("p (k t) -> p k t", k=KC), ACT.Copy).then_inc(xhi_ready, 1)

            def take_logits(i, q, at):
                sc.wait_ge(aux_ready, at)
                nc.scalar.activation(logits[:, :, 0:NE], aux[:].rearrange("p (j e) -> p j e", j=NT),
                                     ACT.Copy).then_inc(logits_ready, 1)

            high(0, 0)
            for w in range(3):
                sc.wait_ge(rec_loaded[w], 16)
                nc.scalar.activation(rec_hi[:, w], rec_st[:, w], ACT.Copy).then_inc(rechi_ready, 1)
            take_logits(0, 0, 1)
            sc.wait_ge(sha_loaded, 16)
            nc.scalar.activation(sha_hi[:], sha_st[:], ACT.Copy).then_inc(rechi_ready, 1)
            with sc.Fori(0, PAIRS) as i:
                for p in range(2):
                    def unit_act(j, u):
                        sc.wait_ge(gate_ready[u], count(i, p, NT, j + 1))
                        if j > 0:
                            sc.wait_ge(basis_ready[u], count(i, p, NT, j))
                        nc.scalar.activation(act[u][:], gate_ps[u][:], ACT.Silu).then_inc(act_ready[u], 1)

                    def take_mixedT(j):
                        sc.wait_ge(aux_ready, aux_at(i, p, mix_use(j)))
                        nc.scalar.activation(mixedT[:], aux[:, 0:P], ACT.Copy).then_inc(mixedT_ready, 1)

                    sc.wait_ge(negmax_ready, count(i, p, 1, 1))
                    for j in range(NT):
                        nc.scalar.activation(expd[:, j], logits[:, j, 0:NE], ACT.Exp, bias=negmax[:, j:j + 1],
                                             accum_out=expsum[:, j:j + 1]).then_inc(exp_ready, 1)
                    for d in range(DC):
                        f_b, i_b, g_b = (0, 1, 0) if d == 0 else (1, 0, 1)
                        f_k, i_k, g_k = (1, 1, 2) if d == 0 else (2, 3, 3)
                        sc.wait_ge(wide_ready[f_b], count(i, p, WIDE, f_k + 1))
                        nc.scalar.activation(th[:, d], wide[f_b][:], ACT.Tanh, scale=0.5).then_inc(th_ready, 1)
                        sc.wait_ge(wide_ready[i_b], count(i, p, WIDE, i_k + 1))
                        nc.scalar.activation(si[:, d], wide[i_b][:], ACT.Silu).then_inc(si_ready, 1)
                        sc.wait_ge(wide_ready[g_b], count(i, p, WIDE, g_k + 1))
                        nc.scalar.activation(gs[:, d], wide[g_b][:], ACT.Silu).then_inc(gs_ready, 1)
                        sc.wait_ge(state_ready, count(i, p, DC, d + 1))
                        nc.scalar.activation(state2[:, d], state[:, d], ACT.Square).then_inc(state2_ready, 1)
                        if d == 1:
                            sc.wait_ge(aux_ready, aux_at(i, p, CHOSEN_USE))
                            nc.scalar.activation(chosenT[:], aux[:], ACT.Copy).then_inc(chosenT_ready, 1)
                    for d in range(DC):
                        sc.wait_ge(wide_ready[0], count(i, p, WIDE, 4 + d + 1))
                        nc.scalar.activation(sha_act[:, d], wide[0][:], ACT.Silu).then_inc(shaact_ready, 1)
                    unit_act(0, 0)
                    unit_act(0, 1)
                    unit_act(1, 0)
                    take_mixedT(0)
                    unit_act(1, 1)
                    unit_act(2, 0)
                    take_mixedT(1)
                    high(i, p + 1)
                    unit_act(2, 1)
                    unit_act(3, 0)
                    take_mixedT(2)
                    unit_act(3, 1)
                    take_logits(i, p + 1, aux_at(i, p, ROUTER_USE))
                    take_mixedT(3)

        @block.vector
        def _(dve):
            def stats(i, q):
                nth = i + 1 + q // 2
                dve.wait_ge(x_loaded[q % 2], nth * 16)
                for j in range(NT):
                    nc.vector.bn_stats(bn[:, j], x_sb[q % 2][:, j]).then_inc(bn_ready, 1)
                wait_apart(dve, bn_ready, count(i, q, NT, NT))
                for j in range(NT):
                    nc.vector.bn_aggr(mv[:, j], bn[:, j]).then_inc(mv_ready, 1)

            def low(i, q, h):
                s = slice(h * T // 2, (h + 1) * T // 2)
                dve.wait_ge(xhi_ready, count(i, q, 2, h + 1))
                nc.vector.tensor_tensor(xT_lo[q % 2][:, :, s], wide[h][:].rearrange("p (k t) -> p k t", k=KC),
                                        xT_hi[q % 2][:, :, s].bitcast(fp32), ALU.subtract).then_inc(xlo_ready, 1)

            nc.vector.memset(logits[:, :, NE:LW], PAD).then_inc(consts_ready, 1)
            nc.vector.memset(keys[:, :, TOPK:NQ], PAD).then_inc(consts_ready, 1)
            nc.vector.memset(ones[:], 1.0).then_inc(consts_ready, 1)
            nc.vector.memset(mixw[:, NK:NK + 1], 1.0).then_inc(consts_ready, 1)
            stats(0, 0)
            dve.wait_ge(small_loaded[0], 16)
            nc.vector.tensor_tensor(amp2[:], amps_sb[:], amps_sb[:], ALU.mult).then_inc(mixw_steps, 1)
            dve.wait_ge(mixw_steps, 1)
            nc.vector.tensor_tensor(power[:], amp2[:, :, 0], amp2[:, :, 1], ALU.add).then_inc(mixw_steps, 1)
            dve.wait_ge(mixw_steps, 2)
            nc.vector.reduce_sum(psum_all[:], power[:], axis=AX.X).then_inc(mixw_steps, 1)
            dve.wait_ge(mixw_steps, 3)
            nc.vector.tensor_scalar(pinv[:], psum_all[:], FFN_EPS, None, ALU.add).then_inc(mixw_steps, 1)
            dve.wait_ge(mixw_steps, 4)
            nc.vector.reciprocal(escaled[:], pinv[:]).then_inc(mixw_steps, 1)
            dve.wait_ge(mixw_steps, 5)
            dve.wait_ge(small_loaded[1], 16)
            nc.vector.tensor_scalar(mixw[:, 0:NK], power[:], escaled[:], escale_sb[:], ALU.mult,
                                    ALU.mult).then_inc(mixw_steps, 1)
            for w in range(3):
                dve.wait_ge(rechi_ready, w + 1)
                nc.vector.tensor_tensor(rec_lo[:, w], rec_st[:, w], rec_hi[:, w].bitcast(fp32),
                                        ALU.subtract).then_inc(reclo_ready, 1)
                if w == 0:
                    low(0, 0, 0)
                    low(0, 0, 1)
            dve.wait_ge(rechi_ready, 4)
            nc.vector.tensor_tensor(sha_lo[:], sha_st[:], sha_hi[:].bitcast(fp32), ALU.subtract).then_inc(reclo_ready, 1)
            dve.wait_ge(small_loaded[2], 16)

            with dve.Fori(0, PAIRS) as i:
                for p in range(2):
                    wait_apart(dve, logits_ready, count(i, p, 1, 1))
                    for j in range(NT):
                        nc.vector.max(top8[:, j], logits[:, j, 0:NE]).then_inc(top8_ready, 1)
                    dve.wait_ge(top8_ready, count(i, p, NT, NT))
                    nc.vector.tensor_scalar(negmax[:], top8[:, :, 0], -1.0, None, ALU.mult).then_inc(negmax_ready, 1)
                    nc.vector.tensor_copy(keys[:, :, 0:TOPK], top8[:, :, 0:TOPK]).then_inc(keys_ready, 1)
                    wait_apart(dve, keys_ready, count(i, p, 1, 1))
                    for j in range(NT):
                        nc.vector.match_replace(marked[:, j], keys[:, j], logits[:, j], MARK).then_inc(marked_ready, 1)
                    for d in range(DC):
                        dve.wait_ge(th_ready, count(i, p, DC, d + 1))
                        nc.vector.tensor_scalar(decay[:, d], th[:, d], 0.5, 0.5, ALU.mult, ALU.add).then_inc(decay_ready, 1)
                        dve.wait_ge(si_ready, count(i, p, DC, d + 1))
                        nc.vector.scalar_tensor_tensor(inflow[:, d], th[:, d], -1.0, si[:, d], ALU.add,
                                                       ALU.mult).then_inc(inflow_ready, 1)
                        dve.wait_ge(decay_ready, count(i, p, DC, d + 1))
                        dve.wait_ge(inflow_ready, count(i, p, DC, d + 1))
                        nc.vector.tensor_tensor_scan(state[:, d], decay[:, d], inflow[:, d], 0.0, ALU.mult,
                                                     ALU.add).then_inc(state_ready, 1)
                        if d == 0:
                            dve.wait_ge(marked_ready, count(i, p, NT, NT))
                            dve.wait_ge(exp_ready, count(i, p, NT, NT))
                            nc.vector.scalar_tensor_tensor(chosen[:], marked[:, :, 0:NE], MARK, expd[:], ALU.is_equal,
                                                           ALU.mult).then_inc(chosen_ready, 1)
                        dve.wait_ge(gs_ready, count(i, p, DC, d + 1))
                        dve.wait_ge(state_ready, count(i, p, DC, d + 1))
                        nc.vector.scalar_tensor_tensor(gated[:, d], gs[:, d], gnorm_sb[:, d:d + 1], state[:, d], ALU.mult,
                                                       ALU.mult).then_inc(gated_ready, 1)
                    for d in range(DC):
                        dve.wait_ge(wide_ready[1], count(i, p, WIDE, 4 + d + 1))
                        dve.wait_ge(shaact_ready, count(i, p, DC, d + 1))
                        nc.vector.tensor_tensor(sha[:, d], sha_act[:, d], wide[1][:], ALU.mult).then_inc(sha_ready, 1)
                        if d == 0:
                            dve.wait_ge(aux_ready, aux_at(i, p, COEF_USE))
                            sums = aux[:, 0:NT * 16].rearrange("p (j c) -> p j c", j=NT)
                            nc.vector.scalar_tensor_tensor(den[:], expsum[:], FFN_EPS, sums[:, :, NK], ALU.mult,
                                                           ALU.add).then_inc(den_ready, 1)
                            dve.wait_ge(den_ready, count(i, p, 1, 1))
                            nc.vector.reciprocal(deninv[:], den[:]).then_inc(deninv_ready, 1)
                            dve.wait_ge(deninv_ready, count(i, p, 1, 1))
                            nc.vector.tensor_tensor(coef[:], sums[:, :, 0:NK],
                                                    deninv[:].rearrange("p (j o) -> p j o", o=1).to_broadcast([P, NT, NK]),
                                                    ALU.mult).then_inc(coef_ready, 1)

                    def mix(j, u):
                        dve.wait_ge(up_ready[u], count(i, p, NT, j + 1))
                        dve.wait_ge(act_ready[u], count(i, p, NT, j + 1))
                        nc.vector.tensor_tensor(basis[u][:], act[u][:], up_ps[u][:], ALU.mult).then_inc(basis_ready[u], 1)
                        dve.wait_ge(basis_ready[u], count(i, p, NT, j + 1))
                        if j == 0 and u == 0:
                            dve.wait_ge(coef_ready, count(i, p, 1, 1))
                        m = mixed[j % 2]
                        for k in range(UK):
                            kk = u * UK + k
                            c = coef[:, j, kk:kk + 1]
                            if kk == 0:
                                nc.vector.tensor_scalar(m[:], basis[u][:, 0:P], c, None, ALU.mult).then_inc(mix_steps, 1)
                            else:
                                dve.wait_ge(mix_steps, count(i, p, MIX, NK * j + kk))
                                nc.vector.scalar_tensor_tensor(m[:], basis[u][:, k * P:(k + 1) * P], c, m[:], ALU.mult,
                                                               ALU.add).then_inc(mix_steps, 1)

                    def finish(j):
                        dve.wait_ge(proj_ready, count(i, p, NT, j + 1))
                        if j == 0:
                            dve.wait_ge(rscale_ready, count(i, p, 1, 1))
                        dve.wait_ge(out_stored[j], (i * 2 + (p + 1)) * 16)
                        nc.vector.scalar_tensor_tensor(out_sb[j][:], proj[:, 0:H], rscale[:, j:j + 1], x_sb[p][:, j], ALU.mult,
                                                       ALU.add).then_inc(resid_ready, 1)
                        dve.wait_ge(resid_ready, count(i, p, NT, j + 1))
                        nc.vector.tensor_tensor(out_sb[j][:], out_sb[j][:], proj[:, H:2 * H], ALU.add).then_inc(out_ready, 1)

                    mix(0, 0)
                    mix(0, 1)
                    dve.wait_ge(aux_ready, aux_at(i, p, SUMSQ_USE))
                    nc.vector.tensor_scalar(meansq[:], aux[:, 0:NT], 0.25 / H, RMS_EPS, ALU.mult, ALU.add).then_inc(meansq_ready, 1)
                    stats(i, p + 1)
                    mix(1, 0)
                    mix(1, 1)
                    finish(0)
                    mix(2, 0)
                    low(i, p + 1, 0)
                    low(i, p + 1, 1)
                    mix(2, 1)
                    finish(1)
                    mix(3, 0)
                    mix(3, 1)
                    finish(2)
                    finish(3)

        @block.tensor
        def _(pe):
            def split_product(ps, l_hi, l_lo, r_hi, r_lo):
                last = None
                n = 0
                for k in range(KC):
                    for a, b in ((l_hi(k), r_hi(k)), (l_hi(k), r_lo(k)), (l_lo(k), r_hi(k))):
                        last = nc.tensor.matmul(ps, a, b, start=(n == 0), stop=(n == 3 * KC - 1))
                        n += 1
                return last

            def transposes(i, q):
                for h in range(2):
                    if h == 0:
                        pe.wait_ge(xn_ready, count(i, q, NT, 2))
                    else:
                        pe.wait_ge(xn_ready, count(i, q, NT, NT))
                    for k in range(KC):
                        for t in range(2):
                            c = (k * 2 + t) * P
                            last = nc.tensor.transpose(wide[h][:, c:c + P], xn[:, 2 * h + t, k * P:(k + 1) * P], ident[:])
                    last.then_inc(wide_ready[h], 1)

            def router(i, q):
                pe.wait_ge(xT_ready, count(i, q, 2, 2))
                for j in range(NT):
                    for k in range(KC):
                        last = nc.tensor.matmul(aux[:, j * NE:(j + 1) * NE], xT[:, k, j * P:(j + 1) * P], router_sb[:, k],
                                                start=(k == 0), stop=(k == KC - 1))
                last.then_inc(aux_ready, 1)

            pe.wait_ge(ident_ready, 2)
            transposes(0, 0)
            pe.wait_ge(router_loaded, 16)
            router(0, 0)
            pe.wait_ge(consts_ready, 4)
            pe.wait_ge(mixw_steps, 6)
            with pe.Fori(0, PAIRS) as i:
                for p in range(2):
                    def channels(bank, w_hi, w_lo):
                        split_product(wide[bank][:], w_hi, w_lo, lambda k: xT_hi[p][:, k], lambda k: xT_lo[p][:, k]
                                      ).then_inc(wide_ready[bank], 1)

                    def recurrence(w, d, bank):
                        pe.wait_ge(reclo_ready, w + 1)
                        s = slice(d * P, (d + 1) * P)
                        channels(bank, lambda k: rec_hi[:, w, k, s], lambda k: rec_lo[:, w, k, s])

                    def shared(w, d, bank):
                        pe.wait_ge(reclo_ready, 4)
                        s = slice(w * H + d * P, w * H + (d + 1) * P)
                        channels(bank, lambda k: sha_hi[:, k, s], lambda k: sha_lo[:, k, s])

                    def unit(j, u):
                        s = slice(j * P, (j + 1) * P)
                        for n, (ps, ready, used) in enumerate(((gate_ps, gate_ready, act_ready), (up_ps, up_ready, basis_ready))):
                            w = 2 * u + n
                            pe.wait_ge(roulo_ready, w + 1)
                            if j > 0:
                                pe.wait_ge(used[u], count(i, p, NT, j))
                            split_product(ps[u][:], lambda k: xT_hi[p][:, k, s], lambda k: xT_lo[p][:, k, s],
                                          lambda k: rou_hi[:, w, k], lambda k: rou_lo[:, w, k]).then_inc(ready[u], 1)

                    def mix_transpose(j):
                        pe.wait_ge(mix_steps, count(i, p, MIX, NK * (j + 1)))
                        nc.tensor.transpose(aux[:, 0:P], mixed[j % 2][:], ident[:]).then_inc(aux_ready, 1)

                    def project(j):
                        s = slice(j * P, (j + 1) * P)
                        if j == 0:
                            pe.wait_ge(down_loaded, 16)
                            pe.wait_ge(gated_ready, count(i, p, DC, DC))
                        else:
                            pe.wait_ge(out_ready, count(i, p, NT, j))
                        for d in range(DC):
                            nc.tensor.matmul(proj[:, 0:H], gated[:, d, s], down_sb[:, d], start=(d == 0), stop=(d == DC - 1))
                        for d in range(DC):
                            nc.tensor.matmul(proj[:, H:2 * H], sha[:, d, s], down_sb[:, DC + d], start=(d == 0), stop=False)
                        pe.wait_ge(mixedT_ready, count(i, p, NT, j + 1))
                        nc.tensor.matmul(proj[:, H:2 * H], mixedT[:], down_sb[:, 2 * DC], start=False,
                                         stop=True).then_inc(proj_ready, 1)

                    pe.wait_ge(xlo_ready, count(i, p, 2, 2))
                    recurrence(0, 0, 0)
                    recurrence(1, 0, 1)
                    pe.wait_ge(th_ready, count(i, p, DC, 1))
                    recurrence(2, 0, 0)
                    pe.wait_ge(si_ready, count(i, p, DC, 1))
                    recurrence(0, 1, 1)
                    pe.wait_ge(gs_ready, count(i, p, DC, 1))
                    recurrence(1, 1, 0)
                    pe.wait_ge(th_ready, count(i, p, DC, 2))
                    recurrence(2, 1, 1)
                    pe.wait_ge(chosen_ready, count(i, p, 1, 1))
                    for j in range(NT):
                        last = nc.tensor.transpose(aux[:, j * P:(j + 1) * P], chosen[:, j], ident[:])
                    last.then_inc(aux_ready, 1)
                    pe.wait_ge(si_ready, count(i, p, DC, 2))
                    shared(0, 0, 0)
                    pe.wait_ge(gs_ready, count(i, p, DC, 2))
                    shared(1, 0, 1)
                    pe.wait_ge(chosenT_ready, count(i, p, 1, 1))
                    for j in range(NT):
                        last = nc.tensor.matmul(aux[:, j * 16:j * 16 + NK + 1], chosenT[:, j * P:(j + 1) * P], mixw[:],
                                                start=True, stop=True)
                    last.then_inc(aux_ready, 1)
                    pe.wait_ge(shaact_ready, count(i, p, DC, 1))
                    shared(0, 1, 0)
                    pe.wait_ge(sha_ready, count(i, p, DC, 1))
                    shared(1, 1, 1)
                    unit(0, 0)
                    unit(0, 1)
                    pe.wait_ge(coef_ready, count(i, p, 1, 1))
                    pe.wait_ge(state2_ready, count(i, p, DC, DC))
                    for j in range(NT):
                        for d in range(DC):
                            last = nc.tensor.matmul(aux[:, j:j + 1], state2[:, d, j * P:(j + 1) * P], ones[:],
                                                    start=(d == 0), stop=(d == DC - 1))
                    last.then_inc(aux_ready, 1)
                    unit(1, 0)
                    pe.wait_ge(meansq_ready, count(i, p, 1, 1))
                    mix_transpose(0)
                    unit(1, 1)
                    pe.wait_ge(sha_ready, count(i, p, DC, 2))
                    project(0)
                    unit(2, 0)
                    mix_transpose(1)
                    pe.wait_ge(shaact_ready, count(i, p, DC, 2))
                    transposes(i, p + 1)
                    unit(2, 1)
                    project(1)
                    unit(3, 0)
                    mix_transpose(2)
                    unit(3, 1)
                    project(2)
                    router(i, p + 1)
                    pe.wait_ge(logits_ready, count(i, p + 1, 1, 1))
                    mix_transpose(3)
                    project(3)


def _chunks(w):
    return w.reshape(-1, P, w.shape[1]).transpose(1, 0, 2)


def kernel(**inputs):
    import numpy as _np
    import concourse.bacc as _bacc
    from concourse import mybir as _mybir
    from concourse.bass_utils import run_bass_kernel_spmd as _run

    a = {k: _np.asarray(v) for k, v in inputs.items()}
    wg, wu = a["L0_ffn_w_gate"], a["L0_ffn_w_up"]
    half = wg.shape[1] // 2
    arrays = {
        "x": a["L0_attn_hidden_states"],
        "router_w": _chunks(a["L0_ffn_w_router"]),
        "rec_w": _np.stack([_chunks(a[n].T) for n in ("L0_attn_Wf", "L0_attn_Wi", "L0_attn_Wg")]),
        "shared_w": _chunks(_np.concatenate([a["L0_ffn_shared_w_gate"], a["L0_ffn_shared_w_up"]], axis=1)),
        "routed_w": _np.stack([_chunks(w[:, u * half:(u + 1) * half]) for u in range(2) for w in (wg, wu)]),
        "down_w": _chunks(_np.concatenate([a["L0_attn_Wo"].T, a["L0_ffn_shared_w_down"], a["L0_ffn_w_down"]], axis=0)),
        "gnorm": a["L0_attn_gnorm_w"].reshape(-1, P).T,
        "amps": a["L0_ffn_amplitudes"].reshape(a["L0_ffn_amplitudes"].shape[0], -1),
        "escale": a["L0_ffn_expert_scale"].reshape(-1, 1),
    }
    arrays = {k: _np.ascontiguousarray(v) for k, v in arrays.items()}
    nc = _bacc.Bacc("TRN2", target_bir_lowering=False, num_devices=1)
    args = [nc.dram_tensor(n, v.shape, _mybir.dt.from_np(v.dtype), kind="ExternalInput").ap() for n, v in arrays.items()]
    shape = a["L0_attn_hidden_states"].shape
    args.append(nc.dram_tensor("out", shape, _mybir.dt.float32, kind="ExternalOutput").ap())
    layer_kernel(nc, *args)
    r = _run(nc, [arrays], core_ids=[0])
    return r.results[0]["out"]
```

```python
from contextlib import ExitStack

import concourse.bass as bass
from concourse import mybir

P = 128


def layer_kernel(nc, x, router_w, rec_w, shared_w, routed_w, down_w, gnorm, amps, escale, out):
    fp32 = mybir.dt.float32
    fp32r = mybir.dt.float32r
    ALU = mybir.AluOpType
    ACT = mybir.ActivationFunctionType
    AX = mybir.AxisListType

    NB, T, H = x.shape
    NT = T // P
    KC = H // P
    DC = H // P
    NE = amps.shape[0]
    NK = amps.shape[1] // 2
    TOPK = 4
    UK = NK // 2
    FW = UK * P
    NU = 2
    NQ = TOPK * 2
    LW = NE + NQ - TOPK
    PAD = -3.0e38
    MARK = 3.0e38
    LN_EPS, RMS_EPS, FFN_EPS = 1e-5, 1e-5, 1e-8
    PAIRS = NB // 2
    WARM_UP = 31
    assert PAIRS == 2 and NT == 4 and KC == 2 and DC == 2 and NE == P and T == 512

    ctx = ExitStack()
    with ctx:
        def sb(name, shape, dt=fp32):
            return ctx.enter_context(nc.sbuf_tensor(name, shape, dt))

        def pb(name):
            return ctx.enter_context(nc.psum_tensor(name, [P, 512], fp32))

        def sem(name):
            return ctx.enter_context(nc.semaphore(name))

        ident = sb("ident", [P, P])
        router_sb = sb("router_sb", [P, KC, NE])
        rec_st = sb("rec_st", [P, 3, KC, H])
        rec_hi = sb("rec_hi", [P, 3, KC, H], fp32r)
        rec_lo = sb("rec_lo", [P, 3, KC, H], fp32r)
        sha_st = sb("sha_st", [P, KC, 2 * H])
        sha_hi = sb("sha_hi", [P, KC, 2 * H], fp32r)
        sha_lo = sb("sha_lo", [P, KC, 2 * H], fp32r)
        rou_st = sb("rou_st", [P, 2 * NU, KC, FW])
        rou_hi = sb("rou_hi", [P, 2 * NU, KC, FW], fp32r)
        rou_lo = sb("rou_lo", [P, 2 * NU, KC, FW], fp32r)
        down_st = sb("down_st", [P, 2 * DC + 1, H])
        down_hi = sb("down_hi", [P, 2 * DC + 1, H], fp32r)
        down_lo = sb("down_lo", [P, 2 * DC + 1, H], fp32r)
        gnorm_sb = sb("gnorm_sb", [P, DC])
        amps_sb = sb("amps_sb", [P, NK, 2])
        escale_sb = sb("escale_sb", [P, 1])
        amp2 = sb("amp2", [P, NK, 2])
        power = sb("power", [P, NK])
        psum_all = sb("psum_all", [P, 1])
        pinv = sb("pinv", [P, 1])
        escaled = sb("escaled", [P, 1])
        mixw = sb("mixw", [P, NK + 1])
        ones = sb("ones", [P, 1])
        neghalf = sb("neghalf", [P, NT])

        x_sb = [sb(f"x_sb{p}", [P, NT, H]) for p in range(2)]
        bn = sb("bn", [P, NT, 6])
        mv = sb("mv", [P, NT, 2])
        negmean = sb("negmean", [P, NT])
        vareps = sb("vareps", [P, NT])
        rstd = sb("rstd", [P, NT])
        xn = sb("xn", [P, NT, H])
        xT_hi = [sb(f"xT_hi{p}", [P, KC, T], fp32r) for p in range(2)]
        xT_lo = [sb(f"xT_lo{p}", [P, KC, T], fp32r) for p in range(2)]
        xT = sb("xT", [P, KC, T])
        logits = sb("logits", [P, NT, LW])
        marked = sb("marked", [P, NT, LW])
        top8 = sb("top8", [P, NT, NQ])
        keys = sb("keys", [P, NT, NQ])
        negmax = sb("negmax", [P, NT])
        expd = sb("expd", [P, NT, NE])
        expsum = sb("expsum", [P, NT])
        chosen = sb("chosen", [P, NT, NE])
        chosenT = sb("chosenT", [P, T])
        den = sb("den", [P, NT])
        deninv = sb("deninv", [P, NT])
        coef = sb("coef", [P, NT, NK])
        th = sb("th", [P, DC, T])
        decay = sb("decay", [P, DC, T])
        si = sb("si", [P, DC, T])
        inflow = si
        state = sb("state", [P, DC, T])
        state2 = sb("state2", [P, DC, T])
        gs = sb("gs", [P, DC, T])
        sumsq = state2[:, 0]
        gated = decay
        gated_hi = sb("gated_hi", [P, DC, T], fp32r)
        gated_lo = sb("gated_lo", [P, DC, T], fp32r)
        meansq = sb("meansq", [P, NT])
        rpow = sb("rpow", [P, NT])
        rscale = sb("rscale", [P, NT])
        sha_act = sb("sha_act", [P, DC, T])
        sha = sha_act
        sha_h = sb("sha_h", [P, DC, T], fp32r)
        sha_l = sb("sha_l", [P, DC, T], fp32r)
        act = [sb(f"act{u}", [P, FW]) for u in range(NU)]
        basis = [sb(f"basis{u}", [P, FW]) for u in range(NU)]
        mixed = [sb(f"mixed{j}", [P, P]) for j in range(2)]
        mixedT_hi = sb("mixedT_hi", [P, P], fp32r)
        mixedT_lo = sb("mixedT_lo", [P, P], fp32r)
        out_sb = [sb(f"out_sb{j}", [P, H]) for j in range(NT)]

        wide = [pb("wide0"), pb("wide1")]
        gate_ps = [pb(f"gate_ps{u}") for u in range(NU)]
        up_ps = [pb(f"up_ps{u}") for u in range(NU)]
        aux = pb("aux")
        proj = pb("proj")
        rec_ps = [proj[:, 0:H]] * (NT - 1) + [gate_ps[0][:, 0:H]]
        ffn_ps = [proj[:, H:2 * H]] * (NT - 1) + [up_ps[0][:, 0:H]]

        x_loaded = [sem(f"x_loaded{p}") for p in range(2)]
        x_half_loaded = sem("x_half_loaded")
        router_loaded = sem("router_loaded")
        rec_loaded = [sem(f"rec_loaded{w}") for w in range(3)]
        sha_loaded = sem("sha_loaded")
        rou_loaded = [sem(f"rou_loaded{w}") for w in range(2 * NU)]
        down_loaded = sem("down_loaded")
        small_loaded = [sem(f"small_loaded{w}") for w in range(3)]
        consts_ready = sem("consts_ready")
        ident_ready = sem("ident_ready")
        neghalf_ready = sem("neghalf_ready")
        waited_apart = sem("waited_apart")
        rechi_ready = sem("rechi_ready")
        reclo_ready = sem("reclo_ready")
        rouhi_ready = sem("rouhi_ready")
        roulo_ready = sem("roulo_ready")
        mixw_steps = sem("mixw_steps")
        bn_ready = sem("bn_ready")
        mv_ready = sem("mv_ready")
        moments_ready = sem("moments_ready")
        rstd_ready = sem("rstd_ready")
        xn_ready = sem("xn_ready")
        xhi_ready = sem("xhi_ready")
        xlo_ready = sem("xlo_ready")
        xT_ready = sem("xT_ready")
        wide_ready = [sem("wide0_ready"), sem("wide1_ready")]
        aux_ready = sem("aux_ready")
        logits_ready = sem("logits_ready")
        top8_ready = sem("top8_ready")
        keys_ready = sem("keys_ready")
        negmax_ready = sem("negmax_ready")
        marked_ready = sem("marked_ready")
        exp_ready = sem("exp_ready")
        chosen_ready = sem("chosen_ready")
        chosenT_ready = sem("chosenT_ready")
        den_ready = sem("den_ready")
        deninv_ready = sem("deninv_ready")
        coef_ready = sem("coef_ready")
        th_ready = sem("th_ready")
        decay_ready = sem("decay_ready")
        si_ready = sem("si_ready")
        inflow_ready = sem("inflow_ready")
        state_ready = sem("state_ready")
        state2_ready = sem("state2_ready")
        gs_ready = sem("gs_ready")
        gated_ready = sem("gated_ready")
        gatedhi_ready = sem("gatedhi_ready")
        gatedlo_ready = sem("gatedlo_ready")
        sumsq_ready = sem("sumsq_ready")
        meansq_ready = sem("meansq_ready")
        rpow_ready = sem("rpow_ready")
        rscale_ready = sem("rscale_ready")
        shaact_ready = sem("shaact_ready")
        sha_ready = sem("sha_ready")
        shah_ready = sem("shah_ready")
        shal_ready = sem("shal_ready")
        downhi_ready = sem("downhi_ready")
        downlo_ready = sem("downlo_ready")
        gate_ready = [sem(f"gate_ready{u}") for u in range(NU)]
        up_ready = [sem(f"up_ready{u}") for u in range(NU)]
        act_ready = [sem(f"act_ready{u}") for u in range(NU)]
        basis_ready = [sem(f"basis_ready{u}") for u in range(NU)]
        mix_steps = sem("mix_steps")
        mixedThi_ready = sem("mixedThi_ready")
        mixedTlo_ready = sem("mixedTlo_ready")
        proj_ready = sem("proj_ready")
        resid_ready = sem("resid_ready")
        out_ready = sem("out_ready")
        out_stored = [sem(f"out_stored{j}") for j in range(NT)]

        def count(i, p, n, k):
            return i * (2 * n) + (p * n + k)

        MIX = NK * NT
        WIDE = (7, 6)
        FORGET_AT, INPUT_AT, OUTGATE_AT = ((1, 1), (0, 1)), ((1, 2), (1, 3)), ((0, 2), (0, 3))
        SHGATE_AT, SHUP_AT, NEXT_X_USE, NEXT_ROUTER_USE = ((1, 4), (1, 5)), ((0, 4), (0, 5)), 6, 7
        AUX = 7
        CHOSEN_USE, COEF_USE, SUMSQ_USE, MIX_USE = 1, 2, 3, 4

        def wide_at(i, p, bank, use):
            return count(i, p, WIDE[bank], 1 + use)

        def aux_at(i, p, use):
            return count(i, p, AUX, 1 + use)

        x_v = x.rearrange("b (j p) h -> b p j h", p=P)
        out_v = out.rearrange("b (j p) h -> b j p h", p=P)

        def wait_apart(eng, semaphore, value):
            eng.wait_ge(semaphore, value)
            eng.sem_inc(waited_apart, 1)

        block = ctx.enter_context(nc.Block())

        @block.sync
        def _(sp):
            sp.dma_start(x_sb[0][:, 0:NT // 2], x_v[0][:, 0:NT // 2]).then_inc(x_half_loaded, 16)
            for w in range(3):
                sp.dma_start(rec_st[:, w], rec_w[w]).then_inc(rec_loaded[w], 16)
            sp.dma_start(router_sb[:], router_w).then_inc(router_loaded, 16)
            sp.dma_start(sha_st[:], shared_w).then_inc(sha_loaded, 16)
            for w in range(2 * NU):
                sp.dma_start(rou_st[:, w], routed_w[w]).then_inc(rou_loaded[w], 16)
            sp.dma_start(down_st[:], down_w).then_inc(down_loaded, 16)
            for j in range(NT):
                sp.sem_inc(out_stored[j], 16)
            with sp.Fori(0, PAIRS) as i:
                for p in range(2):
                    sp.wait_ge(gated_ready, count(i, p, DC, 1))
                    nxt = i * 2 + 1 if p == 0 else (i * -2) + (NB - 2)
                    sp.dma_start(x_sb[1 - p][:], x_v[nxt]).then_inc(x_loaded[1 - p], 16)
                    for j in range(NT):
                        sp.wait_ge(out_ready, count(i, p, NT, j + 1))
                        sp.dma_start(out_v[i * 2 + p, j], out_sb[j][:]).then_inc(out_stored[j], 16)
            for j in range(NT):
                sp.wait_ge(out_stored[j], 16 * (NB + 1))
            sp.wait_ge(x_loaded[0], 16 * (PAIRS + 1))

        @block.gpsimd
        def _(pool):
            nc.gpsimd.memset(ident[:], 0.0).then_inc(ident_ready, 1)
            nc.gpsimd.memset(neghalf[:], -0.5).then_inc(neghalf_ready, 1)
            pool.wait_ge(ident_ready, 1)
            nc.gpsimd.affine_select(out=ident[:], in_=ident[:], compare_op=ALU.not_equal, fill=1.0, base=0,
                                    pattern=[[-1, P]], channel_multiplier=1).then_inc(ident_ready, 1)
            pool.wait_ge(neghalf_ready, 1)

            def inverse_deviation(i, q):
                pool.wait_ge(moments_ready, count(i, q, 2, 1))
                nc.gpsimd.tensor_tensor(rstd[:], vareps[:], neghalf[:], ALU.pow).then_inc(rstd_ready, 1)

            def normalise(i, q):
                pool.wait_ge(moments_ready, count(i, q, 2, 2))
                wait_apart(pool, rstd_ready, count(i, q, 1, 1))
                for j in range(NT):
                    nc.gpsimd.tensor_scalar(xn[:, j], x_sb[q % 2][:, j], negmean[:, j:j + 1], rstd[:, j:j + 1],
                                            ALU.add, ALU.mult).then_inc(xn_ready, 1)

            def join(i, q):
                for h in range(2):
                    pool.wait_ge(xlo_ready, count(i, q, 2, h + 1))
                    s = slice(h * T // 2, (h + 1) * T // 2)
                    nc.gpsimd.tensor_tensor(xT[:, :, s], xT_hi[q % 2][:, :, s].bitcast(fp32),
                                            xT_lo[q % 2][:, :, s].bitcast(fp32), ALU.add).then_inc(xT_ready, 1)

            def low_part(lo, whole, hi, done):
                nc.gpsimd.tensor_tensor(lo, whole, hi.bitcast(fp32), ALU.subtract).then_inc(done, 1)

            inverse_deviation(0, 0)
            for w in range(2 * NU):
                pool.wait_ge(rou_loaded[w], 16)
                nc.gpsimd.tensor_scalar(rou_hi[:, w], rou_st[:, w], 1.0, 0.0, ALU.mult, ALU.add).then_inc(rouhi_ready, 1)
                pool.wait_ge(rouhi_ready, w + 1)
                low_part(rou_lo[:, w], rou_st[:, w], rou_hi[:, w], roulo_ready)
            pool.wait_ge(down_loaded, 16)
            nc.gpsimd.tensor_scalar(down_hi[:], down_st[:], 1.0, 0.0, ALU.mult, ALU.add).then_inc(downhi_ready, 1)
            pool.wait_ge(downhi_ready, 1)
            low_part(down_lo[:], down_st[:], down_hi[:], downlo_ready)
            with pool.Fori(0, PAIRS) as i:
                for p in range(2):
                    for d in range(DC):
                        pool.wait_ge(gatedhi_ready, count(i, p, DC, d + 1))
                        low_part(gated_lo[:, d], gated[:, d], gated_hi[:, d], gatedlo_ready)
                    pool.wait_ge(state2_ready, count(i, p, DC, DC))
                    nc.gpsimd.tensor_tensor(sumsq, state2[:, 0], state2[:, 1], ALU.add).then_inc(sumsq_ready, 1)
                    for d in range(DC):
                        pool.wait_ge(shah_ready, count(i, p, DC, d + 1))
                        low_part(sha_l[:, d], sha[:, d], sha_h[:, d], shal_ready)
                    pool.wait_ge(meansq_ready, count(i, p, 1, 1))
                    nc.gpsimd.tensor_tensor(rpow[:], meansq[:], neghalf[:], ALU.pow).then_inc(rpow_ready, 1)
                    wait_apart(pool, rpow_ready, count(i, p, 1, 1))
                    nc.gpsimd.tensor_scalar(rscale[:], rpow[:], -0.5, 0.0, ALU.mult, ALU.add).then_inc(rscale_ready, 1)
                    inverse_deviation(i, p + 1)
                    normalise(i, p + 1)
                    join(i, p + 1)

        @block.scalar
        def _(sc):
            sc.dma_start(x_sb[0][:, NT // 2:], x_v[0][:, NT // 2:]).then_inc(x_loaded[0], 16)
            sc.dma_start(amps_sb[:], amps.rearrange("e (k c) -> e k c", c=2)).then_inc(small_loaded[0], 16)
            sc.dma_start(escale_sb[:], escale).then_inc(small_loaded[1], 16)
            sc.dma_start(gnorm_sb[:], gnorm).then_inc(small_loaded[2], 16)

            def high(q, at):
                for h in range(2):
                    sc.wait_ge(wide_ready[h], at[h])
                    nc.scalar.activation(xT_hi[q][:, :, h * T // 2:(h + 1) * T // 2],
                                         wide[h][:].rearrange("p (k t) -> p k t", k=KC), ACT.Copy).then_inc(xhi_ready, 1)

            def take_logits(ps, ready, at):
                sc.wait_ge(ready, at)
                nc.scalar.activation(logits[:, :, 0:NE], ps[:].rearrange("p (j e) -> p j e", j=NT),
                                     ACT.Copy).then_inc(logits_ready, 1)

            for w in range(3):
                sc.wait_ge(rec_loaded[w], 16)
                nc.scalar.activation(rec_hi[:, w], rec_st[:, w], ACT.Copy).then_inc(rechi_ready, 1)
            for h in range(2):
                sc.wait_ge(wide_ready[h], 1)
                nc.scalar.activation(xT[:, :, h * T // 2:(h + 1) * T // 2],
                                     wide[h][:].rearrange("p (k t) -> p k t", k=KC), ACT.Copy).then_inc(xT_ready, 1)
            sc.wait_ge(sha_loaded, 16)
            nc.scalar.activation(sha_hi[:], sha_st[:], ACT.Copy).then_inc(rechi_ready, 1)
            take_logits(aux, aux_ready, 1)
            with sc.Fori(0, PAIRS) as i:
                for p in range(2):
                    def unit_act(j, u):
                        sc.wait_ge(gate_ready[u], count(i, p, NT, j + 1))
                        if j > 0:
                            sc.wait_ge(basis_ready[u], count(i, p, NT, j))
                        nc.scalar.activation(act[u][:], gate_ps[u][:], ACT.Silu).then_inc(act_ready[u], 1)

                    def take_mixedT(j):
                        sc.wait_ge(aux_ready, aux_at(i, p, MIX_USE + j))
                        nc.scalar.activation(mixedT_hi[:], aux[:, 0:P], ACT.Copy).then_inc(mixedThi_ready, 1)

                    sc.wait_ge(negmax_ready, count(i, p, 1, 1))
                    for d in range(DC):
                        for j in range(d * NT // DC, (d + 1) * NT // DC):
                            nc.scalar.activation(expd[:, j], logits[:, j, 0:NE], ACT.Exp, bias=negmax[:, j:j + 1],
                                                 accum_out=expsum[:, j:j + 1]).then_inc(exp_ready, 1)
                        b, use = FORGET_AT[d]
                        sc.wait_ge(wide_ready[b], wide_at(i, p, b, use))
                        nc.scalar.activation(th[:, d], wide[b][:], ACT.Tanh, scale=0.5).then_inc(th_ready, 1)
                    for d in range(DC):
                        b, use = INPUT_AT[d]
                        sc.wait_ge(wide_ready[b], wide_at(i, p, b, use))
                        nc.scalar.activation(si[:, d], wide[b][:], ACT.Silu).then_inc(si_ready, 1)
                        b, use = OUTGATE_AT[d]
                        sc.wait_ge(wide_ready[b], wide_at(i, p, b, use))
                        nc.scalar.activation(gs[:, d], wide[b][:], ACT.Silu).then_inc(gs_ready, 1)
                        sc.wait_ge(state_ready, count(i, p, DC, d + 1))
                        nc.scalar.activation(state2[:, d], state[:, d], ACT.Square).then_inc(state2_ready, 1)
                    sc.wait_ge(aux_ready, aux_at(i, p, CHOSEN_USE))
                    nc.scalar.activation(chosenT[:], aux[:], ACT.Copy).then_inc(chosenT_ready, 1)
                    for d in range(DC):
                        sc.wait_ge(gated_ready, count(i, p, DC, d + 1))
                        nc.scalar.activation(gated_hi[:, d], gated[:, d], ACT.Copy).then_inc(gatedhi_ready, 1)
                        b, use = SHGATE_AT[d]
                        sc.wait_ge(wide_ready[b], wide_at(i, p, b, use))
                        nc.scalar.activation(sha_act[:, d], wide[b][:], ACT.Silu).then_inc(shaact_ready, 1)
                    for d in range(DC):
                        sc.wait_ge(sha_ready, count(i, p, DC, d + 1))
                        nc.scalar.activation(sha_h[:, d], sha[:, d], ACT.Copy).then_inc(shah_ready, 1)
                    unit_act(0, 0)
                    unit_act(0, 1)
                    unit_act(1, 0)
                    take_mixedT(0)
                    unit_act(1, 1)
                    unit_act(2, 0)
                    take_mixedT(1)
                    high(1 - p, [wide_at(i, p, h, NEXT_X_USE) for h in range(2)])
                    unit_act(2, 1)
                    unit_act(3, 0)
                    take_mixedT(2)
                    unit_act(3, 1)
                    take_mixedT(3)
                    take_logits(wide[0], wide_ready[0], wide_at(i, p, 0, NEXT_ROUTER_USE))

        @block.vector
        def _(dve):
            def stats(i, q):
                nth = i + 1 + q // 2
                if q > 0:
                    dve.wait_ge(x_loaded[q % 2], nth * 16)
                for j in range(NT):
                    if q == 0 and j == 0:
                        dve.wait_ge(x_half_loaded, 16)
                    if q == 0 and j == NT // 2:
                        dve.wait_ge(x_loaded[0], 16)
                    nc.vector.bn_stats(bn[:, j], x_sb[q % 2][:, j]).then_inc(bn_ready, 1)
                wait_apart(dve, bn_ready, count(i, q, NT, NT))
                for j in range(NT):
                    nc.vector.bn_aggr(mv[:, j], bn[:, j]).then_inc(mv_ready, 1)
                dve.wait_ge(mv_ready, count(i, q, NT, NT))
                nc.vector.tensor_scalar(vareps[:], mv[:, :, 1], LN_EPS, None, ALU.add).then_inc(moments_ready, 1)
                nc.vector.tensor_scalar(negmean[:], mv[:, :, 0], -1.0, None, ALU.mult).then_inc(moments_ready, 1)

            def low(i, q, h):
                s = slice(h * T // 2, (h + 1) * T // 2)
                dve.wait_ge(xhi_ready, count(i, q, 2, h + 1))
                nc.vector.tensor_tensor(xT_lo[q % 2][:, :, s], wide[h][:].rearrange("p (k t) -> p k t", k=KC),
                                        xT_hi[q % 2][:, :, s].bitcast(fp32), ALU.subtract).then_inc(xlo_ready, 1)

            def find(i, q):
                wait_apart(dve, logits_ready, count(i, q, 1, 1))
                for j in range(NT):
                    nc.vector.max(top8[:, j], logits[:, j, 0:NE]).then_inc(top8_ready, 1)
                dve.wait_ge(top8_ready, count(i, q, NT, NT))
                nc.vector.tensor_scalar(negmax[:], top8[:, :, 0], -1.0, None, ALU.mult).then_inc(negmax_ready, 1)
                nc.vector.tensor_copy(keys[:, :, 0:TOPK], top8[:, :, 0:TOPK]).then_inc(keys_ready, 1)

            def mark(i, q):
                wait_apart(dve, keys_ready, count(i, q, 1, 1))
                for j in range(NT):
                    nc.vector.match_replace(marked[:, j], keys[:, j], logits[:, j], MARK).then_inc(marked_ready, 1)

            nc.vector.memset(logits[:, :, NE:LW], PAD).then_inc(consts_ready, 1)
            nc.vector.memset(keys[:, :, TOPK:NQ], PAD).then_inc(consts_ready, 1)
            nc.vector.memset(ones[:], 1.0).then_inc(consts_ready, 1)
            nc.vector.memset(mixw[:, NK:NK + 1], 1.0).then_inc(consts_ready, 1)
            stats(0, 0)
            dve.wait_ge(small_loaded[0], 16)
            nc.vector.tensor_tensor(amp2[:], amps_sb[:], amps_sb[:], ALU.mult).then_inc(mixw_steps, 1)
            dve.wait_ge(mixw_steps, 1)
            nc.vector.tensor_tensor(power[:], amp2[:, :, 0], amp2[:, :, 1], ALU.add).then_inc(mixw_steps, 1)
            dve.wait_ge(mixw_steps, 2)
            nc.vector.reduce_sum(psum_all[:], power[:], axis=AX.X).then_inc(mixw_steps, 1)
            dve.wait_ge(mixw_steps, 3)
            nc.vector.tensor_scalar(pinv[:], psum_all[:], FFN_EPS, None, ALU.add).then_inc(mixw_steps, 1)
            dve.wait_ge(mixw_steps, 4)
            nc.vector.reciprocal(escaled[:], pinv[:]).then_inc(mixw_steps, 1)
            dve.wait_ge(mixw_steps, 5)
            dve.wait_ge(small_loaded[1], 16)
            nc.vector.tensor_scalar(mixw[:, 0:NK], power[:], escaled[:], escale_sb[:], ALU.mult,
                                    ALU.mult).then_inc(mixw_steps, 1)
            dve.wait_ge(rstd_ready, 1)
            dve.wait_ge(moments_ready, 2)
            for j in range(NT):
                nc.vector.tensor_scalar(xn[:, j], x_sb[0][:, j], negmean[:, j:j + 1], rstd[:, j:j + 1],
                                        ALU.add, ALU.mult).then_inc(xn_ready, 1)
            for w in range(3):
                dve.wait_ge(rechi_ready, w + 1)
                nc.vector.tensor_tensor(rec_lo[:, w], rec_st[:, w], rec_hi[:, w].bitcast(fp32),
                                        ALU.subtract).then_inc(reclo_ready, 1)
                if w == 0:
                    for h in range(2):
                        s = slice(h * T // 2, (h + 1) * T // 2)
                        dve.wait_ge(xT_ready, h + 1)
                        nc.vector.tensor_copy(xT_hi[0][:, :, s], xT[:, :, s]).then_inc(xhi_ready, 1)
                        dve.wait_ge(xhi_ready, h + 1)
                        nc.vector.tensor_tensor(xT_lo[0][:, :, s], xT[:, :, s], xT_hi[0][:, :, s].bitcast(fp32),
                                                ALU.subtract).then_inc(xlo_ready, 1)
                    find(0, 0)
            mark(0, 0)
            dve.wait_ge(rechi_ready, 4)
            nc.vector.tensor_tensor(sha_lo[:], sha_st[:], sha_hi[:].bitcast(fp32), ALU.subtract).then_inc(reclo_ready, 1)
            dve.wait_ge(small_loaded[2], 16)

            with dve.Fori(0, PAIRS) as i:
                for p in range(2):
                    for d in range(DC):
                        dve.wait_ge(th_ready, count(i, p, DC, d + 1))
                        nc.vector.tensor_scalar(decay[:, d], th[:, d], 0.5, 0.5, ALU.mult, ALU.add).then_inc(decay_ready, 1)
                    for d in range(DC):
                        dve.wait_ge(si_ready, count(i, p, DC, d + 1))
                        nc.vector.scalar_tensor_tensor(inflow[:, d], th[:, d], -1.0, si[:, d], ALU.add,
                                                       ALU.mult).then_inc(inflow_ready, 1)
                        dve.wait_ge(decay_ready, count(i, p, DC, d + 1))
                        dve.wait_ge(inflow_ready, count(i, p, DC, d + 1))
                        nc.vector.tensor_tensor_scan(state[:, d], decay[:, d], inflow[:, d], 0.0, ALU.mult,
                                                     ALU.add).then_inc(state_ready, 1)
                        if d == 0:
                            dve.wait_ge(marked_ready, count(i, p, NT, NT))
                            dve.wait_ge(exp_ready, count(i, p, NT, NT))
                            nc.vector.scalar_tensor_tensor(chosen[:], marked[:, :, 0:NE], MARK, expd[:], ALU.is_equal,
                                                           ALU.mult).then_inc(chosen_ready, 1)
                        dve.wait_ge(gs_ready, count(i, p, DC, d + 1))
                        dve.wait_ge(state_ready, count(i, p, DC, d + 1))
                        nc.vector.scalar_tensor_tensor(gated[:, d], gs[:, d], gnorm_sb[:, d:d + 1], state[:, d], ALU.mult,
                                                       ALU.mult).then_inc(gated_ready, 1)
                    for d in range(DC):
                        b, use = SHUP_AT[d]
                        dve.wait_ge(wide_ready[b], wide_at(i, p, b, use))
                        dve.wait_ge(shaact_ready, count(i, p, DC, d + 1))
                        nc.vector.tensor_tensor(sha[:, d], sha_act[:, d], wide[b][:], ALU.mult).then_inc(sha_ready, 1)
                        if d == 0:
                            dve.wait_ge(aux_ready, aux_at(i, p, COEF_USE))
                            sums = aux[:, 0:NT * 16].rearrange("p (j c) -> p j c", j=NT)
                            nc.vector.scalar_tensor_tensor(den[:], expsum[:], FFN_EPS, sums[:, :, NK], ALU.mult,
                                                           ALU.add).then_inc(den_ready, 1)
                            dve.wait_ge(den_ready, count(i, p, 1, 1))
                            nc.vector.reciprocal(deninv[:], den[:]).then_inc(deninv_ready, 1)
                            dve.wait_ge(deninv_ready, count(i, p, 1, 1))
                            nc.vector.tensor_tensor(coef[:], sums[:, :, 0:NK],
                                                    deninv[:].rearrange("p (j o) -> p j o", o=1).to_broadcast([P, NT, NK]),
                                                    ALU.mult).then_inc(coef_ready, 1)

                    def mix(j, u):
                        dve.wait_ge(up_ready[u], count(i, p, NT, j + 1))
                        dve.wait_ge(act_ready[u], count(i, p, NT, j + 1))
                        nc.vector.tensor_tensor(basis[u][:], act[u][:], up_ps[u][:], ALU.mult).then_inc(basis_ready[u], 1)
                        dve.wait_ge(basis_ready[u], count(i, p, NT, j + 1))
                        if j == 0 and u == 0:
                            dve.wait_ge(coef_ready, count(i, p, 1, 1))
                        m = mixed[j % 2]
                        for k in range(UK):
                            kk = u * UK + k
                            c = coef[:, j, kk:kk + 1]
                            if kk == 0:
                                nc.vector.tensor_scalar(m[:], basis[u][:, 0:P], c, None, ALU.mult).then_inc(mix_steps, 1)
                            else:
                                dve.wait_ge(mix_steps, count(i, p, MIX, NK * j + kk))
                                nc.vector.scalar_tensor_tensor(m[:], basis[u][:, k * P:(k + 1) * P], c, m[:], ALU.mult,
                                                               ALU.add).then_inc(mix_steps, 1)

                    def mixed_low(j):
                        dve.wait_ge(mixedThi_ready, count(i, p, NT, j + 1))
                        nc.vector.tensor_tensor(mixedT_lo[:], aux[:, 0:P], mixedT_hi[:].bitcast(fp32),
                                                ALU.subtract).then_inc(mixedTlo_ready, 1)

                    def residual(j):
                        dve.wait_ge(proj_ready, count(i, p, NT + 1, j + 1))
                        if j == 0:
                            dve.wait_ge(rscale_ready, count(i, p, 1, 1))
                        dve.wait_ge(out_stored[j], (i * 2 + (p + 1)) * 16)
                        nc.vector.scalar_tensor_tensor(out_sb[j][:], rec_ps[j], rscale[:, j:j + 1], x_sb[p][:, j], ALU.mult,
                                                       ALU.add).then_inc(resid_ready, 1)

                    def finish(j):
                        if j == NT - 1:
                            dve.wait_ge(proj_ready, count(i, p, NT + 1, NT + 1))
                        dve.wait_ge(resid_ready, count(i, p, NT, j + 1))
                        nc.vector.tensor_tensor(out_sb[j][:], out_sb[j][:], ffn_ps[j], ALU.add).then_inc(out_ready, 1)

                    stats(i, p + 1)
                    mix(0, 0)
                    mix(0, 1)
                    dve.wait_ge(aux_ready, aux_at(i, p, SUMSQ_USE))
                    nc.vector.tensor_scalar(meansq[:], aux[:, 0:NT], 0.25 / H, RMS_EPS, ALU.mult, ALU.add).then_inc(meansq_ready, 1)
                    mix(1, 0)
                    mixed_low(0)
                    mix(1, 1)
                    residual(0)
                    finish(0)
                    mix(2, 0)
                    mixed_low(1)
                    low(i, p + 1, 0)
                    low(i, p + 1, 1)
                    mix(2, 1)
                    residual(1)
                    finish(1)
                    mix(3, 0)
                    mixed_low(2)
                    mix(3, 1)
                    residual(2)
                    finish(2)
                    mixed_low(3)
                    residual(3)
                    find(i, p + 1)
                    finish(3)
                    mark(i, p + 1)

        @block.tensor
        def _(pe):
            def split_product(ps, l_hi, l_lo, r_hi, r_lo):
                last = None
                n = 0
                for k in range(KC):
                    for a, b in ((l_hi(k), r_hi(k)), (l_hi(k), r_lo(k)), (l_lo(k), r_hi(k))):
                        last = nc.tensor.matmul(ps, a, b, start=(n == 0), stop=(n == 3 * KC - 1))
                        n += 1
                return last

            def parts_product(ps, chunks, start, stop):
                last = None
                terms = [(a, w[:, c]) for hi, lo, c in chunks for a, w in ((hi, down_hi), (hi, down_lo), (lo, down_hi))]
                for n, (a, b) in enumerate(terms):
                    last = nc.tensor.matmul(ps, a, b, start=(start and n == 0), stop=(stop and n == len(terms) - 1))
                return last

            def transposes(i, q):
                for h in range(2):
                    if h == 0:
                        pe.wait_ge(xn_ready, count(i, q, NT, 2))
                    else:
                        pe.wait_ge(xn_ready, count(i, q, NT, NT))
                    for k in range(KC):
                        for t in range(2):
                            c = (k * 2 + t) * P
                            last = nc.tensor.transpose(wide[h][:, c:c + P], xn[:, 2 * h + t, k * P:(k + 1) * P], ident[:])
                    last.then_inc(wide_ready[h], 1)

            def router(i, q, ps, ready):
                for j in range(NT):
                    if j % 2 == 0:
                        pe.wait_ge(xT_ready, count(i, q, 2, j // 2 + 1))
                    for k in range(KC):
                        last = nc.tensor.matmul(ps[:, j * NE:(j + 1) * NE], xT[:, k, j * P:(j + 1) * P], router_sb[:, k],
                                                start=(k == 0), stop=(k == KC - 1))
                last.then_inc(ready, 1)

            pe.wait_ge(ident_ready, 2)
            for _ in range(WARM_UP):
                nc.tensor.transpose(gate_ps[0][:, 0:P], ident[:], ident[:])
            transposes(0, 0)
            pe.wait_ge(router_loaded, 16)
            router(0, 0, aux, aux_ready)
            pe.wait_ge(consts_ready, 4)
            pe.wait_ge(mixw_steps, 6)
            with pe.Fori(0, PAIRS) as i:
                for p in range(2):
                    def channels(bank, w_hi, w_lo):
                        split_product(wide[bank][:], w_hi, w_lo, lambda k: xT_hi[p][:, k], lambda k: xT_lo[p][:, k]
                                      ).then_inc(wide_ready[bank], 1)

                    def recurrence(w, d, at):
                        bank, _ = at
                        pe.wait_ge(reclo_ready, w + 1)
                        s = slice(d * P, (d + 1) * P)
                        channels(bank, lambda k: rec_hi[:, w, k, s], lambda k: rec_lo[:, w, k, s])

                    def shared(w, d, at):
                        bank, _ = at
                        pe.wait_ge(reclo_ready, 4)
                        s = slice(w * H + d * P, w * H + (d + 1) * P)
                        channels(bank, lambda k: sha_hi[:, k, s], lambda k: sha_lo[:, k, s])

                    def unit(j, u):
                        s = slice(j * P, (j + 1) * P)
                        for w in (2 * u, 2 * u + 1):
                            pe.wait_ge(roulo_ready, w + 1)
                        if j > 0:
                            pe.wait_ge(act_ready[u], count(i, p, NT, j))
                            pe.wait_ge(basis_ready[u], count(i, p, NT, j))
                        for k, parts in ((0, (xT_hi[p], xT_lo[p])), (1, (xT_lo[p], xT_hi[p]))):
                            for n, part in enumerate(parts):
                                for w, ps, ready in ((2 * u, gate_ps[u], gate_ready[u]), (2 * u + 1, up_ps[u], up_ready[u])):
                                    rights = (rou_hi, rou_lo) if part is xT_hi[p] else (rou_hi,)
                                    for r in rights:
                                        last = nc.tensor.matmul(ps[:], part[:, k, s], r[:, w, k],
                                                                start=(k == 0 and n == 0 and r is rou_hi),
                                                                stop=(k == KC - 1 and n == 1 and r is rou_lo))
                                    if k == KC - 1 and n == 1:
                                        last.then_inc(ready, 1)

                    def mix_transpose(j):
                        pe.wait_ge(mix_steps, count(i, p, MIX, NK * (j + 1)))
                        nc.tensor.transpose(aux[:, 0:P], mixed[j % 2][:], ident[:]).then_inc(aux_ready, 1)

                    def project(j):
                        s = slice(j * P, (j + 1) * P)
                        if j == 0:
                            pe.wait_ge(downlo_ready, 1)
                            pe.wait_ge(gatedlo_ready, count(i, p, DC, DC))
                        elif j == NT - 1:
                            pe.wait_ge(act_ready[0], count(i, p, NT, NT))
                            pe.wait_ge(basis_ready[0], count(i, p, NT, NT))
                        else:
                            pe.wait_ge(out_ready, count(i, p, NT, j))
                        last = parts_product(rec_ps[j], [(gated_hi[:, d, s], gated_lo[:, d, s], d) for d in range(DC)],
                                             True, True)
                        if j == NT - 1:
                            last.then_inc(proj_ready, 1)
                        if j == 0:
                            pe.wait_ge(shal_ready, count(i, p, DC, DC))
                        parts_product(ffn_ps[j], [(sha_h[:, d, s], sha_l[:, d, s], DC + d) for d in range(DC)], True, False)
                        pe.wait_ge(mixedTlo_ready, count(i, p, NT, j + 1))
                        parts_product(ffn_ps[j], [(mixedT_hi[:], mixedT_lo[:], 2 * DC)], False,
                                      True).then_inc(proj_ready, 1)

                    pe.wait_ge(xlo_ready, count(i, p, 2, 2))
                    recurrence(0, 0, FORGET_AT[0])
                    pe.wait_ge(logits_ready, count(i, p, 1, 1))
                    recurrence(0, 1, FORGET_AT[1])
                    pe.wait_ge(th_ready, count(i, p, DC, 1))
                    recurrence(1, 0, INPUT_AT[0])
                    pe.wait_ge(th_ready, count(i, p, DC, 2))
                    recurrence(2, 0, OUTGATE_AT[0])
                    pe.wait_ge(si_ready, count(i, p, DC, 1))
                    recurrence(1, 1, INPUT_AT[1])
                    pe.wait_ge(gs_ready, count(i, p, DC, 1))
                    recurrence(2, 1, OUTGATE_AT[1])
                    pe.wait_ge(chosen_ready, count(i, p, 1, 1))
                    for j in range(NT):
                        last = nc.tensor.transpose(aux[:, j * P:(j + 1) * P], chosen[:, j], ident[:])
                    last.then_inc(aux_ready, 1)
                    pe.wait_ge(si_ready, count(i, p, DC, 2))
                    shared(0, 0, SHGATE_AT[0])
                    pe.wait_ge(gs_ready, count(i, p, DC, 2))
                    shared(1, 0, SHUP_AT[0])
                    pe.wait_ge(chosenT_ready, count(i, p, 1, 1))
                    for j in range(NT):
                        last = nc.tensor.matmul(aux[:, j * 16:j * 16 + NK + 1], chosenT[:, j * P:(j + 1) * P], mixw[:],
                                                start=True, stop=True)
                    last.then_inc(aux_ready, 1)
                    pe.wait_ge(shaact_ready, count(i, p, DC, 1))
                    shared(0, 1, SHGATE_AT[1])
                    pe.wait_ge(sha_ready, count(i, p, DC, 1))
                    shared(1, 1, SHUP_AT[1])
                    unit(0, 0)
                    unit(0, 1)
                    pe.wait_ge(coef_ready, count(i, p, 1, 1))
                    pe.wait_ge(sumsq_ready, count(i, p, 1, 1))
                    for j in range(NT):
                        last = nc.tensor.matmul(aux[:, j:j + 1], sumsq[:, j * P:(j + 1) * P], ones[:], start=True, stop=True)
                    last.then_inc(aux_ready, 1)
                    unit(1, 0)
                    pe.wait_ge(meansq_ready, count(i, p, 1, 1))
                    mix_transpose(0)
                    unit(1, 1)
                    pe.wait_ge(sha_ready, count(i, p, DC, 2))
                    project(0)
                    unit(2, 0)
                    mix_transpose(1)
                    pe.wait_ge(shaact_ready, count(i, p, DC, 2))
                    transposes(i, p + 1)
                    unit(2, 1)
                    project(1)
                    unit(3, 0)
                    mix_transpose(2)
                    unit(3, 1)
                    project(2)
                    router(i, p + 1, wide[0], wide_ready[0])
                    mix_transpose(3)
                    project(3)


def _chunks(w):
    return w.reshape(-1, P, w.shape[1]).transpose(1, 0, 2)


def kernel(**inputs):
    import numpy as _np
    import concourse.bacc as _bacc
    from concourse import mybir as _mybir
    from concourse.bass_utils import run_bass_kernel_spmd as _run

    a = {k: _np.asarray(v) for k, v in inputs.items()}
    wg, wu = a["L0_ffn_w_gate"], a["L0_ffn_w_up"]
    half = wg.shape[1] // 2
    arrays = {
        "x": a["L0_attn_hidden_states"],
        "router_w": _chunks(a["L0_ffn_w_router"]),
        "rec_w": _np.stack([_chunks(a[n].T) for n in ("L0_attn_Wf", "L0_attn_Wi", "L0_attn_Wg")]),
        "shared_w": _chunks(_np.concatenate([a["L0_ffn_shared_w_gate"], a["L0_ffn_shared_w_up"]], axis=1)),
        "routed_w": _np.stack([_chunks(w[:, u * half:(u + 1) * half]) for u in range(2) for w in (wg, wu)]),
        "down_w": _chunks(_np.concatenate([a["L0_attn_Wo"].T, a["L0_ffn_shared_w_down"], a["L0_ffn_w_down"]], axis=0)),
        "gnorm": a["L0_attn_gnorm_w"].reshape(-1, P).T,
        "amps": a["L0_ffn_amplitudes"].reshape(a["L0_ffn_amplitudes"].shape[0], -1),
        "escale": a["L0_ffn_expert_scale"].reshape(-1, 1),
    }
    arrays = {k: _np.ascontiguousarray(v) for k, v in arrays.items()}
    nc = _bacc.Bacc("TRN2", target_bir_lowering=False, num_devices=1)
    args = [nc.dram_tensor(n, v.shape, _mybir.dt.from_np(v.dtype), kind="ExternalInput").ap() for n, v in arrays.items()]
    shape = a["L0_attn_hidden_states"].shape
    args.append(nc.dram_tensor("out", shape, _mybir.dt.float32, kind="ExternalOutput").ap())
    layer_kernel(nc, *args)
    r = _run(nc, [arrays], core_ids=[0])
    return r.results[0]["out"]
```
